# Optimizing a Trainium2 kernel written in Bass

```python
import numpy as np
import jax
import jax.numpy as jnp

def _softmax(x, axis=-1):
    return jax.nn.softmax(x, axis=axis)

def _gelu(x):
    return jax.nn.gelu(x, approximate=True)

def _silu(x):
    return jax.nn.silu(x)

def _sigmoid(x):
    return jax.nn.sigmoid(x)

def _layernorm(x, axis=-1, eps=1e-05):
    m = jnp.mean(x, axis=axis, keepdims=True)
    v = jnp.var(x, axis=axis, keepdims=True)
    return (x - m) / jnp.sqrt(v + eps)

def _scatter_add(tgt, idx, src, axis=0):
    return tgt.at[idx].add(src)

def _segment_sum(src, seg, n):
    return jax.ops.segment_sum(src, seg, n)
kernel_name = 'mk_vit_tower_postln_d1_tok_img1024_r4_fa83e0'

def setup_inputs(seed: int=0):
    np.random.seed(seed)
    _w = jnp.asarray

    def _rec_inputs():
        import jax
        import jax.numpy as jnp
        _rk = jax.random.key(seed)
        x = -0.00016672 + 0.999947 * jax.random.normal(jax.random.fold_in(_rk, 1), (16, 3, 128, 128), jnp.float32)
        return x
    x = _rec_inputs()

    def _L0_tok_setup():
        import jax, jax.numpy as jnp
        import numpy as np
        PATCH = 16

        def _patchify(img):
            B, C, H, Wd = img.shape
            nh, nw = (H // PATCH, Wd // PATCH)
            x = img.reshape(B, C, nh, PATCH, nw, PATCH)
            x = x.transpose(0, 2, 4, 1, 3, 5)
            return x.reshape(B, nh * nw, C * PATCH * PATCH)
        key = jax.random.key(seed)
        k1, k2, k3 = jax.random.split(key, 3)
        B, C, H, W_ = (64, 3, 96, 96)
        patch_dim = PATCH * PATCH * C
        proj_dim = 256
        img = jax.random.normal(k1, (B, C, H, W_), dtype=jnp.float32)
        W = jax.random.normal(k2, (proj_dim, patch_dim), dtype=jnp.float32) * patch_dim ** (-0.5)
        b = jax.random.normal(k3, (proj_dim,), dtype=jnp.float32) * 0.01
        return {'img': img, 'W': W, 'b': b}
    _L0_tok_all = _L0_tok_setup()
    _L0_tok_in = {k: v for k, v in _L0_tok_all.items() if k in ('W', 'b')}
    del _L0_tok_all

    def _L0_attn_setup():
        import jax, jax.numpy as jnp
        import numpy as np
        T, B, E = (512, 16, 256)
        CDIM = 256
        H = 16
        K = 31

        def _xavier(k, shape):
            fan_out, fan_in = shape
            lim = float(np.sqrt(6.0 / (fan_in + fan_out)))
            return jax.random.uniform(k, shape, jnp.float32, -lim, lim)

        def layer_norm(x, g, b, eps=1e-05):
            m = x.mean(-1, keepdims=True)
            v = ((x - m) ** 2).mean(-1, keepdims=True)
            return (x - m) * jax.lax.rsqrt(v + eps) * g + b

        def dynamic_conv(h, ww, bw):
            Tn, Bn, C = h.shape
            R = C // H
            w = jax.nn.softmax((h @ ww.T + bw).reshape(Tn, Bn, H, K), axis=-1)
            hp = jnp.pad(h.reshape(Tn, Bn, H, R), ((K - 1, 0), (0, 0), (0, 0), (0, 0)))
            acc = jnp.zeros((Tn, Bn, H, R), h.dtype)
            for k in range(K):
                acc = acc + w[:, :, :, k:k + 1] * hp[k:k + Tn]
            return acc.reshape(Tn, Bn, C)
        key = jax.random.key(seed)
        ks = jax.random.split(key, 5)
        return {'x': jax.random.normal(ks[0], (T, B, E), jnp.float32), 'w1': _xavier(ks[1], (CDIM, E)), 'b1': jnp.zeros((CDIM,), jnp.float32), 'ww': _xavier(ks[2], (H * K, CDIM)), 'bw': jnp.zeros((H * K,), jnp.float32), 'w2': _xavier(ks[3], (E, CDIM)), 'b2': jnp.zeros((E,), jnp.float32), 'gamma': jnp.ones((E,), jnp.float32), 'beta': jnp.zeros((E,), jnp.float32)}
    _L0_attn_all = _L0_attn_setup()
    _L0_attn_in = {k: v for k, v in _L0_attn_all.items() if k in ('w1', 'b1', 'ww', 'bw', 'w2', 'b2', 'gamma', 'beta')}
    del _L0_attn_all

    def _L0_ffn_setup():
        import jax, jax.numpy as jnp
        import numpy as np
        HIDDEN = 256
        INNER = 1024

        def _weight_quant(w):
            scale = 1.0 / jnp.clip(jnp.mean(jnp.abs(w)), 1e-05)
            wq = jnp.clip(jnp.round(w * scale), -1.0, 1.0) / scale
            return w + jax.lax.stop_gradient(wq - w)

        def _act_quant(x):
            scale = 127.0 / jnp.clip(jnp.max(jnp.abs(x), axis=-1, keepdims=True), 1e-05)
            xq = jnp.clip(jnp.round(x * scale), -128.0, 127.0) / scale
            return x + jax.lax.stop_gradient(xq - x)

        def _bitlinear(x, w):
            return jnp.einsum('bsi,oi->bso', _act_quant(x), _weight_quant(w))
        key = jax.random.key(seed)
        k0, k1, k2, k3 = jax.random.split(key, 4)
        x = jax.random.normal(k0, (4, 512, HIDDEN), dtype=jnp.float32)
        w_gate = jax.random.normal(k1, (INNER, HIDDEN), dtype=jnp.float32) / np.sqrt(HIDDEN)
        w_up = jax.random.normal(k2, (INNER, HIDDEN), dtype=jnp.float32) / np.sqrt(HIDDEN)
        w_down = jax.random.normal(k3, (HIDDEN, INNER), dtype=jnp.float32) / np.sqrt(INNER)
        return {'x': x, 'w_gate': w_gate, 'w_up': w_up, 'w_down': w_down}
    _L0_ffn_all = _L0_ffn_setup()
    _L0_ffn_in = {k: v for k, v in _L0_ffn_all.items() if k in ('w_gate', 'w_up', 'w_down')}
    del _L0_ffn_all
    return {'x': x, 'L0_tok_W': _L0_tok_in['W'], 'L0_tok_b': _L0_tok_in['b'], 'L0_attn_w1': _L0_attn_in['w1'], 'L0_attn_b1': _L0_attn_in['b1'], 'L0_attn_ww': _L0_attn_in['ww'], 'L0_attn_bw': _L0_attn_in['bw'], 'L0_attn_w2': _L0_attn_in['w2'], 'L0_attn_b2': _L0_attn_in['b2'], 'L0_attn_gamma': _L0_attn_in['gamma'], 'L0_attn_beta': _L0_attn_in['beta'], 'L0_ffn_w_gate': _L0_ffn_in['w_gate'], 'L0_ffn_w_up': _L0_ffn_in['w_up'], 'L0_ffn_w_down': _L0_ffn_in['w_down']}

def reference(x, L0_tok_W, L0_tok_b, L0_attn_w1, L0_attn_b1, L0_attn_ww, L0_attn_bw, L0_attn_w2, L0_attn_b2, L0_attn_gamma, L0_attn_beta, L0_ffn_w_gate, L0_ffn_w_up, L0_ffn_w_down):
    import jax
    import jax.numpy as jnp

    def _L0_tok_ref(img, W, b):
        import jax, jax.numpy as jnp
        import numpy as np
        PATCH = 16

        def _patchify(img):
            B, C, H, Wd = img.shape
            nh, nw = (H // PATCH, Wd // PATCH)
            x = img.reshape(B, C, nh, PATCH, nw, PATCH)
            x = x.transpose(0, 2, 4, 1, 3, 5)
            return x.reshape(B, nh * nw, C * PATCH * PATCH)
        patches = _patchify(img)
        return jnp.einsum('bnd,od->bno', patches, W) + b

    def _L0_attn_ref(x, w1, b1, ww, bw, w2, b2, gamma, beta):
        import jax, jax.numpy as jnp
        import numpy as np
        T, B, E = (512, 16, 256)
        CDIM = 256
        H = 16
        K = 31

        def _xavier(k, shape):
            fan_out, fan_in = shape
            lim = float(np.sqrt(6.0 / (fan_in + fan_out)))
            return jax.random.uniform(k, shape, jnp.float32, -lim, lim)

        def layer_norm(x, g, b, eps=1e-05):
            m = x.mean(-1, keepdims=True)
            v = ((x - m) ** 2).mean(-1, keepdims=True)
            return (x - m) * jax.lax.rsqrt(v + eps) * g + b

        def dynamic_conv(h, ww, bw):
            Tn, Bn, C = h.shape
            R = C // H
            w = jax.nn.softmax((h @ ww.T + bw).reshape(Tn, Bn, H, K), axis=-1)
            hp = jnp.pad(h.reshape(Tn, Bn, H, R), ((K - 1, 0), (0, 0), (0, 0), (0, 0)))
            acc = jnp.zeros((Tn, Bn, H, R), h.dtype)
            for k in range(K):
                acc = acc + w[:, :, :, k:k + 1] * hp[k:k + Tn]
            return acc.reshape(Tn, Bn, C)
        h = x @ w1.T + b1
        h = dynamic_conv(h, ww, bw)
        h = h @ w2.T + b2
        return layer_norm(x + h, gamma, beta)

    def _L0_ffn_ref(x, w_gate, w_up, w_down):
        import jax, jax.numpy as jnp
        import numpy as np
        HIDDEN = 256
        INNER = 1024

        def _weight_quant(w):
            scale = 1.0 / jnp.clip(jnp.mean(jnp.abs(w)), 1e-05)
            wq = jnp.clip(jnp.round(w * scale), -1.0, 1.0) / scale
            return w + jax.lax.stop_gradient(wq - w)

        def _act_quant(x):
            scale = 127.0 / jnp.clip(jnp.max(jnp.abs(x), axis=-1, keepdims=True), 1e-05)
            xq = jnp.clip(jnp.round(x * scale), -128.0, 127.0) / scale
            return x + jax.lax.stop_gradient(xq - x)

        def _bitlinear(x, w):
            return jnp.einsum('bsi,oi->bso', _act_quant(x), _weight_quant(w))
        gate = jax.nn.silu(_bitlinear(x, w_gate))
        up = _bitlinear(x, w_up)
        return _bitlinear(gate * up, w_down)
    h = _L0_tok_ref(x, L0_tok_W, L0_tok_b)
    h = _layernorm(h + _L0_attn_ref(h, L0_attn_w1, L0_attn_b1, L0_attn_ww, L0_attn_bw, L0_attn_w2, L0_attn_b2, L0_attn_gamma, L0_attn_beta), axis=-1)
    h = _layernorm(h + _L0_ffn_ref(h, L0_ffn_w_gate, L0_ffn_w_up, L0_ffn_w_down), axis=-1)
    return h

_drawn_inputs = setup_inputs


def setup_inputs(seed=0):
    import zlib

    import numpy as np

    out = dict(_drawn_inputs(seed))
    spreads = {'L0_attn_b1': (0.0, 0.433),
     'L0_attn_bw': (0.0, 0.8),
     'L0_attn_b2': (0.0, 0.1),
     'L0_attn_gamma': (1.0, 0.2),
     'L0_attn_beta': (0.0, 0.1)}
    factors = {'L0_tok_b': 5.13}
    for name, (base, spread) in spreads.items():
        noise = np.random.default_rng([zlib.crc32(name.encode()), seed]).standard_normal(out[name].shape)
        drawn = base * np.exp(spread * noise) if base else spread * noise
        out[name] = jnp.asarray(drawn.astype(out[name].dtype))
    for name, factor in factors.items():
        out[name] = (out[name] * factor).astype(out[name].dtype)
    return out
```

```python
import numpy as np
import concourse.bass as bass
from concourse import mybir
from contextlib import ExitStack

P = 128
IMAGES, CHANNELS, SIDE, PATCH = 16, 3, 128, 16
GRID = SIDE // PATCH
PATCHES = GRID * GRID
D_PATCH = CHANNELS * PATCH * PATCH
D = 256
HEADS, TAPS = 16, 31
R = D // HEADS
INNER = 1024
TILES = IMAGES * PATCHES // P
KC_PATCH, KC, KC_INNER = D_PATCH // P, D // P, INNER // P
LOGITS = HEADS * TAPS
HALF = INNER // 2
POOL_HEADS = (HEADS // 2,) * TILES
DVE_HEADS = tuple(HEADS - n for n in POOL_HEADS)
SLOTS_FIRST = (0, 6)
TOP_EARLY = 2
WARM_UP, WARM_Y, WARM_Q1, WARM_Q2 = 10, 6, 8, 14
LN_EPS = 1e-5
CLIP_EPS = 1e-5
MAGIC = 12582912.0


def vit_tower(nc, xT_d, tokW_d, w1_d, ww_d, w2_d, wg_d, wu_d, wd_d, cols_d, bias_d, ln_d, out_d):
    f32, bf16 = mybir.dt.float32, mybir.dt.bfloat16
    ALU, ACT, AX = mybir.AluOpType, mybir.ActivationFunctionType, mybir.AxisListType

    ctx = ExitStack()
    with ctx:
        def sb(name, shape, dt=f32):
            return ctx.enter_context(nc.sbuf_tensor(name, shape, dt))

        def sem(name):
            return ctx.enter_context(nc.semaphore(name))

        xT = sb("xT", [P, TILES, KC_PATCH, P])
        tokW = sb("tokW", [P, KC_PATCH, D])
        w1 = sb("w1", [P, KC, D])
        ww = sb("ww", [P, KC, LOGITS])
        w2 = sb("w2", [P, KC, D])
        w_raw = sb("w_raw", [P, 3, KC * INNER])
        bias_cols = sb("bias_cols", [P, 2, KC])
        bias_row = sb("bias_row", [P, LOGITS + D])
        ln_rows = sb("ln_rows", [P, 2, D])
        tokb, b1 = bias_cols[:, 0, :], bias_cols[:, 1, :]
        gamma, beta = ln_rows[:, 0, :], ln_rows[:, 1, :]
        ident = sb("ident", [P, P])
        ones = sb("ones", [P, P])
        ones_bf = sb("ones_bf", [P, P], bf16)
        bias_part = sb("bias_part", [P, 2, LOGITS + D], bf16)
        bias_rest = sb("bias_rest", [P, LOGITS + D])
        bias_mm = sb("bias_mm", [P, LOGITS + D], bf16)
        minus_half = sb("minus_half", [P, 1])
        minus_magic = sb("minus_magic", [P, 1])
        magic = sb("magic", [P, 1])
        abs_sum = sb("abs_sum", [P, 3])
        w_mean = sb("w_mean", [P, 3])
        w_scale = sb("w_scale", [P, 3])
        mean_127 = sb("mean_127", [P, 3])
        w_q = sb("w_q", [P, 3, KC * INNER], bf16)
        h1T = sb("h1T", [P, TILES, KC, P])
        h2T = sb("h2T", [P, KC, PATCHES + TILES * P])
        h1b = sb("h1b", [P, 2, D])
        hist = sb("hist", [P, 2 * TILES, D])
        top = sb("top", [P, 2, HEADS])
        probs = sb("probs", [P, 2, 512])
        total = sb("total", [P, 2, HEADS])
        inv_total = sb("inv_total", [P, 2, HEADS])
        prod = sb("prod", [P, 2 * TILES, max(DVE_HEADS) * R])
        prod_pool = sb("prod_pool", [P, 2 * TILES, max(POOL_HEADS) * R])
        y = sb("y", [P, 2, D])
        yT = sb("yT", [P, 2, KC, P])
        stats = sb("stats", [P, 3, 6])
        mv = sb("mv", [P, 3, 2])
        veps = sb("veps", [P, 3, 1])
        rstd = sb("rstd", [P, 3, 1])
        shift_out = sb("shift_out", [P, 1])
        a1 = sb("a1", [P, D])
        a2 = sb("a2", [P, D])
        centred = sb("centred", [P, 2, D])
        h3 = sb("h3", [P, 3, D])
        q1 = sb("q1", [P, D])
        q1T = sb("q1T", [P, 2, KC, P], bf16)
        sc = sb("sc", [P, 2, 12])
        silu = sb("silu", [P, 2, 2, HALF])
        gu = sb("gu", [P, 2, 2, HALF])
        q2T = sb("q2T", [P, KC_INNER, P], bf16)
        f = sb("f", [P, 3, D])
        res = sb("res", [P, 2, D])

        bank = [ctx.enter_context(nc.psum_tensor(f"bank{i}", [P, 512], f32)) for i in range(8)]
        ps_embed = bank[0][:, 0:D].rearrange("p (k n) -> p k n", k=KC)
        ps_hist = bank[0][:, :].rearrange("p (s c) -> p s c", s=2)
        ps_h2T = bank[1][:, 0:D].rearrange("p (k n) -> p k n", k=KC)
        ps_h1 = bank[1][:, D:2 * D]
        ps_logits = bank[2][:, 0:LOGITS]
        ps_yT = bank[3][:, 0:D].rearrange("p (k n) -> p k n", k=KC)
        ps_q1T = bank[3][:, D:2 * D].rearrange("p (k n) -> p k n", k=KC)
        ps_attn = bank[4][:, 0:D]
        ps_down = bank[4][:, D:2 * D]
        ps_mean = bank[6][:, 0:3]

        def ps_gate(t, half):
            return bank[2][:, :] if (t, half) == (TILES - 1, 1) else bank[5][:, :]

        ps_up = [bank[6][:, :], bank[7][:, :]]
        ps_q2T = [bank[6][:, :], bank[7][:, :]]

        x0_in = sem("x0_in")
        x_in = [sem(f"x_in{t}") for t in range(TILES)]
        tokW_in = [sem("tokW_in0"), sem("tokW_in1")]
        cols_in = sem("cols_in")
        w1_in = sem("w1_in")
        ww_in = sem("ww_in")
        w2_in = sem("w2_in")
        bias_in = sem("bias_in")
        ln_in = sem("ln_in")
        ffn_in = [sem(f"ffn_in{j}") for j in range(3)]
        out_done = [sem("out_done0"), sem("out_done1")]
        embed_ps = sem("embed_ps")
        h2T_ps = sem("h2T_ps")
        hist_ps = sem("hist_ps")
        logits_ps = sem("logits_ps")
        yT_ps = sem("yT_ps")
        attn_ps = sem("attn_ps")
        q1T_ps = sem("q1T_ps")
        gate_ps = sem("gate_ps")
        up_ps = sem("up_ps")
        q2T_ps = sem("q2T_ps")
        down_ps = sem("down_ps")
        mean_ps = sem("mean_ps")
        h1T_ok = sem("h1T_ok")
        h2T_ok = sem("h2T_ok")
        h1_ok = sem("h1_ok")
        hist_ok = sem("hist_ok")
        exp_ok = sem("exp_ok")
        yT_ok = sem("yT_ok")
        q1T_ok = sem("q1T_ok")
        silu_ok = sem("silu_ok")
        q2T_ok = sem("q2T_ok")
        abs_ok = sem("abs_ok")
        q2_ok = sem("q2_ok")
        wround_up = sem("wround_up")
        wq_up_ok = sem("wq_up_ok")
        shifted_ok = sem("shifted_ok")
        inv_ok = sem("inv_ok")
        y_dve_ok = sem("y_dve_ok")
        attn_read = sem("attn_read")
        var_attn = sem("var_attn")
        var_mid = sem("var_mid")
        var_out = sem("var_out")
        centred_ok = sem("centred_ok")
        q1_ok = sem("q1_ok")
        up_read = sem("up_read")
        q2_scale_ok = sem("q2_scale_ok")
        down_read = sem("down_read")
        scale_ok = sem("scale_ok")
        h1b_read = sem("h1b_read")
        last_ok = sem("last_ok")
        q2_last_ok = sem("q2_last_ok")
        q2T_last_ok = sem("q2T_last_ok")
        wclip_gate = sem("wclip_gate")
        wscale_ok = sem("wscale_ok")
        mean_read = sem("mean_read")
        dve_step = sem("dve_step")
        ones_ok = sem("ones_ok")
        const_ok = sem("const_ok")
        bias_ok = sem("bias_ok")
        h1b_ok = sem("h1b_ok")
        res_ok = sem("res_ok")
        h3_ok = sem("h3_ok")
        y_pool_ok = sem("y_pool_ok")
        rstd_attn = sem("rstd_attn")
        rstd_mid = sem("rstd_mid")
        rstd_out = sem("rstd_out")
        wround_down = sem("wround_down")
        wclip_up = sem("wclip_up")
        wclip_down = sem("wclip_down")
        wq_gate_ok = sem("wq_gate_ok")
        wq_down_ok = sem("wq_down_ok")
        pool_step = sem("pool_step")

        block = ctx.enter_context(nc.Block())

        @block.sync
        def _(sp):
            sp.dma_start(tokW[:, 0:3, :], tokW_d[:, 0:3, :]).then_inc(tokW_in[0], 16)
            sp.dma_start(tokW[:, 3:6, :], tokW_d[:, 3:6, :]).then_inc(tokW_in[1], 16)
            sp.dma_start(w1[:], w1_d).then_inc(w1_in, 16)
            sp.dma_start(ww[:], ww_d).then_inc(ww_in, 16)
            sp.dma_start(w_raw[:, 0], wg_d).then_inc(ffn_in[0], 16)
            sp.dma_start(w_raw[:, 1], wu_d).then_inc(ffn_in[1], 16)
            sp.dma_start(xT[:, 2], xT_d[2]).then_inc(x_in[2], 16)
            sp.dma_start(w_raw[:, 2], wd_d).then_inc(ffn_in[2], 16)
            for t in range(3, TILES):
                sp.dma_start(xT[:, t], xT_d[t]).then_inc(x_in[t], 16)
            for t in range(TILES):
                if t < TILES - 1:
                    sp.wait_ge(res_ok, t + 1)
                else:
                    sp.wait_ge(last_ok, 1)
                sp.dma_start(out_d[t * P:(t + 1) * P, :], res[:, t % 2, :]).then_inc(out_done[t % 2], 16)
            for slot in range(2):
                sp.wait_ge(out_done[slot], 16 * TILES // 2)

        @block.tensor
        def _(pe):
            def embed(t):
                if t > 0:
                    pe.wait_ge(x_in[t], 16)
                    pe.wait_ge(hist_ok, t)
                for m in range(KC):
                    for k in range(KC_PATCH):
                        if t == 0 and m == 0 and k in (0, 3):
                            pe.wait_ge(tokW_in[k // 3], 16)
                            pe.wait_ge((x0_in, x_in[0])[k // 3], 16)
                        last = nc.tensor.matmul(ps_embed[:, m, :], tokW[:, k, m * P:(m + 1) * P], xT[:, t, k, :],
                                                start=(k == 0), stop=(k == KC_PATCH - 1))
                last.then_inc(embed_ps, 1)

            def project_in(t):
                if t == 0:
                    pe.wait_ge(w1_in, 16)
                    pe.wait_ge(const_ok, 1)
                pe.wait_ge(h1T_ok, t + 1)
                if t >= 1:
                    pe.wait_ge(h1_ok, t)
                for m in range(KC):
                    for k in range(KC):
                        nc.tensor.matmul(ps_h2T[:, m, :], w1[:, k, m * P:(m + 1) * P], h1T[:, t, k, :],
                                         start=(k == 0), stop=(k == KC - 1))
                for k in range(KC):
                    last = nc.tensor.transpose(ps_h1[:, k * P:(k + 1) * P], h1T[:, t, k, :], ident[:])
                last.then_inc(h2T_ps, 1)

            def logits_start(t):
                if t == 0:
                    pe.wait_ge(ww_in, 16)
                    pe.wait_ge(bias_ok, 1)
                pe.wait_ge(h2T_ok, t + 1)
                if t >= 1:
                    pe.wait_ge(shifted_ok, t)
                nc.tensor.matmul(ps_logits, ones_bf[:], bias_mm[:, 0:LOGITS], start=True, stop=False)
                nc.tensor.matmul(ps_logits, h2T[:, 0, PATCHES + t * P:PATCHES + (t + 1) * P], ww[:, 0, :],
                                 start=False, stop=False)

            def logits_finish(t):
                nc.tensor.matmul(ps_logits, h2T[:, 1, PATCHES + t * P:PATCHES + (t + 1) * P], ww[:, 1, :],
                                 start=False, stop=True).then_inc(logits_ps, 1)

            def history(t):
                pe.wait_ge(h1T_ok, t + 1)
                for s in range(2):
                    for k in range(KC):
                        at = t * P + s * PATCHES
                        last = nc.tensor.transpose(ps_hist[:, s, k * P:(k + 1) * P], h2T[:, k, at:at + P], ident[:])
                last.then_inc(hist_ps, 1)

            def attn_start(t):
                if t == 0:
                    pe.wait_ge(w2_in, 16)
                    pe.wait_ge(bias_ok, 2)
                if t >= 2:
                    pe.wait_ge(down_read, t - 1)
                nc.tensor.matmul(ps_attn, ones_bf[:], bias_mm[:, LOGITS:LOGITS + D], start=True, stop=False)
                for k in range(KC):
                    nc.tensor.matmul(ps_attn[:, k * P:(k + 1) * P], h1T[:, t, k, :], ident[:], start=False, stop=False)
                if t == TILES - 1:
                    pe.wait_ge(hist_ok, TILES)
                    keep_warm(bank[0][:, :], WARM_Y)
                pe.wait_ge(y_dve_ok, t + 1)
                pe.wait_ge(y_pool_ok, t + 1)
                if t >= 1:
                    pe.wait_ge(q1T_ok, t)
                for k in range(KC):
                    last = nc.tensor.transpose(ps_yT[:, k, :], y[:, t % 2, k * P:(k + 1) * P], ident[:])
                last.then_inc(yT_ps, 1)

            def attn_finish(t):
                pe.wait_ge(yT_ok, t + 1)
                for k in range(KC):
                    last = nc.tensor.matmul(ps_attn, yT[:, t % 2, k, :], w2[:, k, :], start=False, stop=(k == KC - 1))
                last.then_inc(attn_ps, 1)

            def in_transposes(t):
                pe.wait_ge(q1_ok, t + 1)
                for k in range(KC):
                    last = nc.tensor.transpose(ps_q1T[:, k, :], q1[:, k * P:(k + 1) * P], ident[:])
                last.then_inc(q1T_ps, 1)

            def gate_up(t):
                if t == 0:
                    pe.wait_ge(wq_gate_ok, 1)
                    pe.wait_ge(wq_up_ok, 1)
                    pe.wait_ge(mean_read, 2)
                pe.wait_ge(q1T_ok, t + 1)
                if t >= 1:
                    pe.wait_ge(silu_ok, 2 * t)
                    pe.wait_ge(q2T_ok, 2 * t)
                order = ((0, 0), (1, 0), (1, 1), (0, 1)) if t < TILES - 1 else ((0, 0), (0, 1), (1, 0), (1, 1))
                for j, half in order:
                    out = (ps_gate(t, half), ps_up[half])[j]
                    if (j, half) == (0, 1) and t < TILES - 1:
                        if t + 2 < TILES:
                            logits_finish(t + 2)
                        pe.wait_ge(silu_ok, 2 * t + 1)
                    elif (j, half) == (0, 1):
                        pe.wait_ge(shifted_ok, TILES)
                    for k in range(KC):
                        at = k * INNER + half * HALF
                        last = nc.tensor.matmul(out, q1T[:, t % 2, k, :], w_q[:, j, at:at + HALF],
                                                start=(k == 0), stop=(k == KC - 1))
                    last.then_inc((gate_ps, up_ps)[j], 1)

            def inner_transposes(t):
                for half in range(2):
                    if t < TILES - 1:
                        pe.wait_ge(q2_ok, 2 * t + 1 + half)
                    elif half == 0:
                        pe.wait_ge(q2_last_ok, 1)
                    else:
                        pe.wait_ge(q2_ok, 2 * t + 1)
                    for k in range(4):
                        last = nc.tensor.transpose(ps_q2T[half][:, k * P:(k + 1) * P],
                                                   gu[:, t % 2, half, k * P:(k + 1) * P], ident[:])
                    last.then_inc(q2T_ps, 1)

            def down(t):
                if t == 0:
                    pe.wait_ge(wq_down_ok, 1)
                pe.wait_ge(attn_read, t + 2 if t + 2 <= TILES else TILES)
                for k in range(KC_INNER):
                    if k in (0, 4):
                        if t < TILES - 1:
                            pe.wait_ge(q2T_ok, 2 * t + 1 + k // 4)
                        elif k == 0:
                            pe.wait_ge(q2T_last_ok, 1)
                        else:
                            pe.wait_ge(q2T_ok, 2 * t + 1)
                    last = nc.tensor.matmul(ps_down, q2T[:, k, :], w_q[:, 2, k * D:(k + 1) * D],
                                            start=(k == 0), stop=(k == KC_INNER - 1))
                last.then_inc(down_ps, 1)

            def keep_warm(out, count):
                for _ in range(count):
                    nc.tensor.matmul(out, ones_bf[:], ones_bf[:, 0:1].broadcast_to([P, 512]), start=True, stop=True)

            pe.wait_ge(ones_ok, 1)
            keep_warm(bank[7][:, :], WARM_UP)
            embed(0)
            project_in(0)
            logits_start(0)
            logits_finish(0)
            history(0)
            embed(1)
            pe.wait_ge(abs_ok, 2)
            nc.tensor.matmul(ps_mean[:, 0:2], ones[:], abs_sum[:, 0:2], start=True, stop=True).then_inc(mean_ps, 1)
            attn_start(0)
            project_in(1)
            attn_finish(0)
            logits_start(1)
            logits_finish(1)
            for i in range(1, TILES + 3):
                if 1 < i <= TILES:
                    attn_start(i - 1)
                if i < TILES:
                    history(i)
                if 1 < i <= TILES:
                    attn_finish(i - 1)
                if i == TILES:
                    keep_warm(bank[0][:, :], WARM_Q1)
                if i + 1 < TILES:
                    embed(i + 1)
                if i == 1:
                    pe.wait_ge(abs_ok, 3)
                    pe.wait_ge(mean_read, 1)
                    nc.tensor.matmul(ps_mean[:, 2:3], ones[:], abs_sum[:, 2:3], start=True,
                                     stop=True).then_inc(mean_ps, 1)
                if i + 1 < TILES:
                    project_in(i + 1)
                if 2 <= i <= TILES + 1:
                    inner_transposes(i - 2)
                if 1 < i and i + 1 < TILES:
                    logits_start(i + 1)
                if i >= TILES and i <= TILES + 1:
                    down(i - 2)
                if i <= TILES:
                    in_transposes(i - 1)
                if i == 1:
                    logits_start(2)
                if 2 <= i < TILES:
                    down(i - 2)
                if i <= TILES:
                    gate_up(i - 1)
                if i == TILES:
                    keep_warm(bank[0][:, :], WARM_Q2)

        @block.scalar
        def _(act):
            def out_h1T(t):
                act.wait_ge(embed_ps, t + 1)
                for m in range(KC):
                    last = nc.scalar.activation(h1T[:, t, m, :], ps_embed[:, m, :], ACT.Identity, bias=tokb[:, m:m + 1])
                last.then_inc(h1T_ok, 1)

            def weight_sum(j):
                act.wait_ge(ffn_in[j], 16)
                nc.scalar.activation(w_q[:, j, :], w_raw[:, j, :], ACT.Abs,
                                     accum_out=abs_sum[:, j:j + 1]).then_inc(abs_ok, 1)

            def weight_round(j, step, done):
                act.wait_ge(wscale_ok, step)
                nc.scalar.activation(w_raw[:, j, :], w_raw[:, j, :], ACT.Identity, bias=magic[:, 0:1],
                                     scale=w_scale[:, j:j + 1]).then_inc(done, 1)

            act.dma_start(xT[:, 0, 0:3], xT_d[0, :, 0:3]).then_inc(x0_in, 16)
            act.dma_start(xT[:, 0, 3:6], xT_d[0, :, 3:6]).then_inc(x_in[0], 16)
            act.dma_start(bias_cols[:], cols_d).then_inc(cols_in, 16)
            act.dma_start(bias_row[0:65, :], bias_d.to_broadcast([65, LOGITS + D])).then_inc(bias_in, 16)
            act.dma_start(xT[:, 1], xT_d[1]).then_inc(x_in[1], 16)
            act.dma_start(ln_rows[:].rearrange("p s c -> p (s c)"), ln_d.to_broadcast([P, 2 * D])).then_inc(ln_in, 16)
            act.dma_start(w2[:], w2_d).then_inc(w2_in, 16)
            nc.scalar.preload_act_table(ACT.Exp)
            act.wait_ge(cols_in, 16)
            act.wait_ge(const_ok, 1)

            def out_h2T(t):
                act.wait_ge(h2T_ps, t + 1)
                for m in range(KC):
                    last = nc.scalar.activation(h2T[:, m, PATCHES + t * P:PATCHES + (t + 1) * P],
                                                ps_h2T[:, m, :], ACT.Identity, bias=b1[:, m:m + 1])
                last.then_inc(h2T_ok, 1)

            def out_h1(t):
                if t >= 2:
                    act.wait_ge(h1b_read, t - 1)
                nc.scalar.copy(h1b[:, t % 2, :], ps_h1).then_inc(h1_ok, 1)

            def out_yT(t):
                act.wait_ge(yT_ps, t + 1)
                if t >= 2:
                    act.wait_ge(attn_ps, t - 1)
                nc.scalar.copy(yT[:, t % 2], ps_yT).then_inc(yT_ok, 1)

            def halves(t):
                return range(2) if t < TILES - 1 else (1,)

            def quant_inner(t):
                act.wait_ge(q2_scale_ok, t + 1)
                for half in halves(t):
                    nc.scalar.activation(gu[:, t % 2, half, :], gu[:, t % 2, half, :], ACT.Identity,
                                         bias=magic[:, 0:1], scale=sc[:, t % 2, 8:9]).then_inc(q2_ok, 1)

            def out_q2T(t):
                for half in halves(t):
                    act.wait_ge(q2T_ps, 2 * t + 1 + half)
                    if t >= 1:
                        act.wait_ge(down_ps, t)
                    nc.scalar.activation(q2T[:, 4 * half:4 * half + 4, :],
                                         ps_q2T[half].rearrange("p (k n) -> p k n", k=4), ACT.Identity,
                                         bias=minus_magic[:, 0:1]).then_inc(q2T_ok, 1)

            def out_hist(t):
                act.wait_ge(hist_ps, t + 1)
                nc.scalar.copy(hist[:, 2 * t:2 * t + 2, :], ps_hist).then_inc(hist_ok, 1)

            def exps(t):
                act.wait_ge(shifted_ok, t + 1)
                nc.scalar.activation(probs[:, t % 2, 0:LOGITS], probs[:, t % 2, 0:LOGITS], ACT.Exp).then_inc(exp_ok, 1)

            def out_q1T(t):
                act.wait_ge(q1T_ps, t + 1)
                if t >= 2:
                    act.wait_ge(gate_ps, 2 * (t - 1))
                nc.scalar.activation(q1T[:, t % 2], ps_q1T, ACT.Identity, bias=minus_magic[:, 0:1]).then_inc(q1T_ok, 1)

            def silus(t):
                act.wait_ge(scale_ok, t + 1)
                if t >= 2:
                    act.wait_ge(up_read, 2 * (t - 1))
                for half in range(2):
                    act.wait_ge(gate_ps, 2 * t + 1 + half)
                    nc.scalar.activation(silu[:, t % 2, half, :], ps_gate(t, half), ACT.Silu,
                                         scale=sc[:, t % 2, 2:3]).then_inc(silu_ok, 1)

            out_h1T(0)
            out_h2T(0)
            out_h1(0)
            weight_sum(0)
            out_hist(0)
            exps(0)
            weight_sum(1)
            out_h1T(1)
            out_yT(0)
            out_h2T(1)
            out_h1(1)
            weight_round(1, 1, wround_up)
            for i in range(1, TILES + 3):
                if 1 < i <= TILES:
                    out_yT(i - 1)
                if i < TILES:
                    out_hist(i)
                if i == 1:
                    exps(1)
                    weight_sum(2)
                    out_h1T(2)
                    act.wait_ge(wclip_up, 1)
                    nc.scalar.activation(w_q[:, 1, :], w_raw[:, 1, :], ACT.Identity,
                                         bias=minus_magic[:, 0:1]).then_inc(wq_up_ok, 1)
                elif i < TILES:
                    nc.scalar.preload_act_table(ACT.Exp)
                    exps(i)
                    nc.scalar.preload_act_table(ACT.Silu)
                if 2 <= i and i + 1 < TILES:
                    out_h1T(i + 1)
                if 2 <= i <= TILES + 1:
                    quant_inner(i - 2)
                if i + 1 < TILES:
                    out_h2T(i + 1)
                if 2 <= i <= TILES + 1:
                    out_q2T(i - 2)
                if i <= TILES:
                    out_q1T(i - 1)
                if i == 1:
                    nc.scalar.preload_act_table(ACT.Silu)
                if i + 1 < TILES:
                    out_h1(i + 1)
                if i <= TILES:
                    silus(i - 1)

        @block.vector
        def _(dve):
            steps = [0]

            def mark(ins):
                steps[0] += 1
                ins.then_inc(dve_step, 1)
                return steps[0]

            def after(step):
                dve.wait_ge(dve_step, step)

            def per_head(ap):
                return ap.rearrange("p (h k) -> p h k", h=HEADS)

            down_scale_step = {}

            def top_logits(t):
                dve.wait_ge(logits_ps, t + 1)
                return mark(nc.vector.tensor_reduce(top[:, t % 2, :], per_head(ps_logits), AX.X, ALU.max))

            def shift(t, step):
                after(step)
                if t >= 2:
                    dve.wait_ge(y_pool_ok, t - 1)
                nc.vector.tensor_tensor(per_head(probs[:, t % 2, 0:LOGITS]), per_head(ps_logits),
                                        top[:, t % 2, :].unsqueeze(2).broadcast_to([P, HEADS, TAPS]),
                                        ALU.subtract).then_inc(shifted_ok, 1)

            def tap_sums(t):
                dve.wait_ge(exp_ok, t + 1)
                return mark(nc.vector.tensor_reduce(total[:, t % 2, :], per_head(probs[:, t % 2, 0:LOGITS]),
                                                    AX.X, ALU.add))

            def tap_inverses(t, step):
                after(step)
                if t >= 2:
                    dve.wait_ge(y_pool_ok, t - 1)
                nc.vector.reciprocal(inv_total[:, t % 2, :], total[:, t % 2, :]).then_inc(inv_ok, 1)

            def first_part(c, o):
                if c is not None:
                    n, heads = 2 * c + 2, DVE_HEADS[c]
                    ch = heads * R
                    if c == 0:
                        tap_inverses(c, tap_sums(c))
                    pr = per_head(probs[:, c % 2, 0:LOGITS])
                    dve.wait_ge(exp_ok, c + 1)
                    dve.wait_ge(hist_ok, c + 1)
                    prod_step = mark(nc.vector.tensor_tensor(
                        prod[:, 0:n, 0:ch].rearrange("p s (h r) -> p s h r", r=R),
                        hist[:, 0:n, 0:ch].rearrange("p s (h r) -> p s h r", r=R),
                        pr[:, 0:heads, TAPS - n:TAPS].rearrange("p h s -> p s h").unsqueeze(3).broadcast_to(
                            [P, n, heads, R]), ALU.mult))
                if o is not None:
                    dve.wait_ge(down_ps, o + 1)
                    after(down_scale_step[o])
                    dve.wait_ge(h3_ok, o + 1)
                    if o >= 3:
                        dve.wait_ge(res_ok, o - 2)
                    nc.vector.scalar_tensor_tensor(f[:, o % 3, :], ps_down, sc[:, o % 2, 9:10], h3[:, o % 3, :],
                                                   ALU.mult, ALU.add).then_inc(down_read, 1)
                if c is not None:
                    after(prod_step)
                    if c >= 2:
                        dve.wait_ge(yT_ps, c - 1)
                    sum_step = mark(nc.vector.tensor_reduce(
                        y[:, c % 2, 0:ch], prod[:, 0:n, 0:ch].rearrange("p s c -> p c s"), AX.X, ALU.add))
                    after(sum_step)
                    dve.wait_ge(inv_ok, c + 1)
                    yv = y[:, c % 2, 0:ch].rearrange("p (h r) -> p h r", r=R)
                    nc.vector.tensor_tensor(yv, yv, inv_total[:, c % 2, 0:heads].unsqueeze(2).broadcast_to(
                        [P, heads, R]), ALU.mult).then_inc(y_dve_ok, 1)

            def out_stats(o):
                dve.wait_ge(down_read, o + 1)
                return mark(nc.vector.bn_stats(stats[:, 2, :], f[:, o % 3, :]))

            def out_variance(o, step):
                after(step)
                if o >= 1:
                    dve.wait_ge(res_ok, o)
                nc.vector.bn_aggr(mv[:, 2, :], stats[:, 2, :]).then_inc(var_out, 1)

            def attn_stats(a):
                dve.wait_ge(attn_ps, a + 1)
                if a == 0:
                    dve.wait_ge(ln_in, 16)
                return mark(nc.vector.bn_stats(stats[:, 0, :], ps_attn))

            def attn_variance(a, step):
                after(step)
                nc.vector.bn_aggr(mv[:, 0, :], stats[:, 0, :]).then_inc(var_attn, 1)

            def attn_centre(a):
                dve.wait_ge(var_attn, a + 1)
                nc.vector.scalar_tensor_tensor(a1[:], ps_attn, mv[:, 0, 0:1], gamma, ALU.subtract,
                                               ALU.mult).then_inc(attn_read, 1)

            def second_part(l, a, g, o):
                sg = sc[:, g % 2, :] if g is not None else None
                alone = a is None
                if alone and o is not None:
                    out_variance(o, out_stats(o))
                for half in range(2):
                    if g is not None:
                        dve.wait_ge(silu_ok, 2 * g + 1 + half)
                        dve.wait_ge(up_ps, 2 * g + 1 + half)
                        if g >= 2:
                            dve.wait_ge(q2T_ps, 2 * (g - 1))
                        nc.vector.tensor_tensor(gu[:, g % 2, half, :], silu[:, g % 2, half, :], ps_up[half],
                                                ALU.mult).then_inc(up_read, 1)
                    if a == 1 and half == 0:
                        dve.wait_ge(wround_down, 1)
                        weight_clip(2, wclip_down)
                    if l is not None and half == (0 if l >= TOP_EARLY else 1):
                        top_step = top_logits(l)
                if l is not None:
                    shift(l, top_step)
                if alone and g is not None:
                    for half in range(2):
                        dve.wait_ge(up_read, 2 * g + 1 + half)
                        abs_step = mark(nc.vector.tensor_reduce(sg[:, 10 + half:11 + half], gu[:, g % 2, half],
                                                                AX.X, ALU.max, apply_absolute_value=True))
                        if half == 0:
                            half_step = abs_step
                    after(half_step)
                    abs_step = mark(nc.vector.tensor_scalar(sg[:, 5:6], sg[:, 10:11], sg[:, 3:4], CLIP_EPS,
                                                            ALU.mult, ALU.max))
                if g is not None and not alone:
                    dve.wait_ge(up_read, 2 * g + 2)
                    abs_step = mark(nc.vector.tensor_reduce(sg[:, 5:6], gu[:, g % 2], AX.XY, ALU.max,
                                                            apply_absolute_value=True))
                if a == 0:
                    dve.wait_ge(wround_up, 1)
                    weight_clip(1, wclip_up)
                if a is not None and a > 0:
                    attn_step = attn_stats(a)
                if g is not None:
                    after(abs_step)
                    if alone:
                        clip_step = mark(nc.vector.scalar_tensor_tensor(sg[:, 6:7], sg[:, 11:12], sg[:, 3:4],
                                                                        sg[:, 5:6], ALU.mult, ALU.max))
                    else:
                        clip_step = mark(nc.vector.tensor_scalar(sg[:, 6:7], sg[:, 5:6], sg[:, 3:4], CLIP_EPS,
                                                                 ALU.mult, ALU.max))
                if a is not None and a > 0:
                    attn_variance(a, attn_step)
                if g is not None:
                    after(clip_step)
                    inv_step = mark(nc.vector.reciprocal(sg[:, 7:8], sg[:, 6:7]))
                if a is not None and a > 0:
                    attn_centre(a)
                if g is not None:
                    after(inv_step)
                    nc.vector.tensor_scalar(sg[:, 8:9], sg[:, 7:8], sg[:, 3:4], 127.0,
                                            ALU.mult, ALU.mult).then_inc(q2_scale_ok, 1)
                    if alone:
                        dve.wait_ge(q2_scale_ok, g + 1)
                        nc.vector.tensor_scalar(gu[:, g % 2, 0, :], gu[:, g % 2, 0, :], sg[:, 8:9], MAGIC,
                                                ALU.mult, ALU.add).then_inc(q2_last_ok, 1)
                        mark(nc.vector.tensor_scalar(sg[:, 9:10], sg[:, 6:7], mean_127[:, 2:3], None, ALU.mult))
                        down_scale_step[g] = steps[0]
                        dve.wait_ge(q2T_ps, 2 * g + 1)
                        dve.wait_ge(down_ps, g)
                        nc.vector.tensor_scalar(q2T[:, 0:4, :], ps_q2T[0].rearrange("p (k n) -> p k n", k=4), -MAGIC,
                                                None, ALU.add).then_inc(q2T_last_ok, 1)
                if o is not None and not alone:
                    out_step = out_stats(o)
                if a is not None:
                    dve.wait_ge(rstd_attn, a + 1)
                    dve.wait_ge(attn_read, a + 1)
                    dve.wait_ge(h1b_ok, a + 1)
                    nc.vector.scalar_tensor_tensor(a2[:], a1[:], rstd[:, 0, 0:1], h1b[:, a % 2, :],
                                                   ALU.mult, ALU.add).then_inc(h1b_read, 1)
                if o is not None and not alone:
                    out_variance(o, out_step)
                if a is not None:
                    dve.wait_ge(h1b_read, a + 1)
                    mid_step = mark(nc.vector.bn_stats(stats[:, 1, :], a2[:]))
                if g is not None and not alone:
                    after(clip_step)
                    down_scale_step[g] = mark(nc.vector.tensor_scalar(sg[:, 9:10], sg[:, 6:7], mean_127[:, 2:3], None,
                                                                      ALU.mult))
                if a is not None:
                    after(mid_step)
                    nc.vector.bn_aggr(mv[:, 1, :], stats[:, 1, :]).then_inc(var_mid, 1)
                    s = sc[:, a % 2, :]
                    if l is not None:
                        total_step = tap_sums(l)
                    dve.wait_ge(var_mid, a + 1)
                    if a >= 2:
                        dve.wait_ge(h3_ok, a - 1)
                    nc.vector.tensor_scalar(centred[:, a % 2, :], a2[:], mv[:, 1, 0:1], None,
                                            ALU.subtract).then_inc(centred_ok, 1)
                    if l is not None:
                        tap_inverses(l, total_step)
                    dve.wait_ge(centred_ok, a + 1)
                    after(mark(nc.vector.tensor_reduce(s[:, 0:1], centred[:, a % 2, :], AX.X, ALU.max,
                                                       apply_absolute_value=True)))
                    dve.wait_ge(rstd_mid, a + 1)
                    after(mark(nc.vector.tensor_scalar(s[:, 1:2], s[:, 0:1], rstd[:, 1, 0:1], CLIP_EPS,
                                                       ALU.mult, ALU.max)))
                    inv_step = mark(nc.vector.reciprocal(s[:, 4:5], s[:, 1:2]))
                    nc.vector.tensor_scalar(s[:, 2:3], s[:, 1:2], mean_127[:, 0:1], None, ALU.mult).then_inc(scale_ok, 1)
                    after(inv_step)
                    scale_step = mark(nc.vector.tensor_scalar(s[:, 7:8], s[:, 4:5], rstd[:, 1, 0:1], 127.0,
                                                              ALU.mult, ALU.mult))
                    mark(nc.vector.tensor_scalar(s[:, 3:4], s[:, 1:2], mean_127[:, 1:2], None, ALU.mult))
                    after(scale_step)
                    if a >= 1:
                        dve.wait_ge(q1T_ps, a)
                    nc.vector.tensor_scalar(q1[:], centred[:, a % 2, :], s[:, 7:8], MAGIC,
                                            ALU.mult, ALU.add).then_inc(q1_ok, 1)

            def last_result(t):
                dve.wait_ge(rstd_out, t + 1)
                dve.wait_ge(out_done[t % 2], 16 * (t // 2))
                nc.vector.tensor_scalar(res[:, t % 2, :], f[:, t % 3, :], mv[:, 2, 0:1], rstd[:, 2, 0:1],
                                        ALU.subtract, ALU.mult).then_inc(last_ok, 1)

            def weight_scales(j0, j1):
                dve.wait_ge(mean_ps, 1 + j0 // 2)
                nc.vector.tensor_scalar(w_mean[:, j0:j1], ps_mean[:, j0:j1], 1.0 / (D * INNER), CLIP_EPS,
                                        ALU.mult, ALU.max).then_inc(mean_read, 1)
                dve.wait_ge(mean_read, 1 + j0 // 2)
                nc.vector.reciprocal(w_scale[:, j0:j1], w_mean[:, j0:j1]).then_inc(wscale_ok, 1)
                mark(nc.vector.tensor_scalar(mean_127[:, j0:j1], w_mean[:, j0:j1], 1.0 / 127.0, None, ALU.mult))

            def weight_round(j):
                dve.wait_ge(wscale_ok, 1)
                after(mark(nc.vector.tensor_scalar(w_raw[:, j, :], w_raw[:, j, :], w_scale[:, j:j + 1], MAGIC,
                                                   ALU.mult, ALU.add)))

            def weight_clip(j, done):
                nc.vector.tensor_scalar(w_raw[:, j, :], w_raw[:, j, :], MAGIC + 1.0, MAGIC - 1.0,
                                        ALU.min, ALU.max).then_inc(done, 1)

            def tile(t):
                return t if 0 <= t < TILES else None

            def bias_rows(lo, hi):
                row, rest, out = bias_row[0:65, lo:hi], bias_rest[0:65, lo:hi], bias_mm[:, lo:hi]
                high, mid = bias_part[0:65, 0, lo:hi], bias_part[0:65, 1, lo:hi]
                high_step = mark(nc.vector.tensor_copy(high, row))
                mark(nc.vector.tensor_copy(out[0:1], row[0:1]))
                after(high_step)
                after(mark(nc.vector.tensor_tensor(rest, row, high, ALU.subtract)))
                mid_step = mark(nc.vector.tensor_copy(mid, rest))
                mark(nc.vector.tensor_copy(out[32:33], rest[32:33]))
                after(mid_step)
                nc.vector.tensor_tensor(out[64:65], rest[64:65], mid[64:65], ALU.subtract).then_inc(bias_ok, 1)

            dve.wait_ge(const_ok, 1)
            dve.wait_ge(bias_in, 16)
            bias_rows(0, LOGITS)
            second_part(0, None, None, None)
            bias_rows(LOGITS, LOGITS + D)
            for i in range(1, TILES + 3):
                first_part(tile(i - 1), tile(i - 3))
                if i == 1:
                    weight_scales(0, 2)
                    weight_round(0)
                    weight_clip(0, wclip_gate)
                    attn_variance(0, attn_stats(0))
                    attn_centre(0)
                second_part(tile(i), tile(i - 1), tile(i - 2), tile(i - 3))
                if i == 1:
                    weight_scales(2, 3)
            last_result(TILES - 1)

        @block.gpsimd
        def _(pool):
            steps = [0]

            def mark(ins):
                steps[0] += 1
                ins.then_inc(pool_step, 1)

            def link(ins):
                mark(ins)
                pool.wait_ge(pool_step, steps[0])

            nc.gpsimd.memset(ones_bf[:], 1.0).then_inc(ones_ok, 1)
            nc.gpsimd.memset(ones[:], 1.0)
            nc.gpsimd.memset(minus_half[:], -0.5)
            nc.gpsimd.memset(minus_magic[:], -MAGIC)
            nc.gpsimd.memset(magic[:], MAGIC)
            nc.gpsimd.memset(h2T[:, :, 0:PATCHES], 0.0)
            nc.gpsimd.memset(bias_mm[:], 0.0)
            link(nc.gpsimd.memset(ident[:], 0.0))
            nc.gpsimd.affine_select(out=ident[:], in_=ident[:], compare_op=ALU.not_equal, fill=1.0, base=0,
                                    pattern=[[-1, P]], channel_multiplier=1).then_inc(const_ok, 1)

            def inv_std(j, var_ready, done, t):
                pool.wait_ge(var_ready, t + 1)
                link(nc.gpsimd.tensor_scalar(veps[:, j, :], mv[:, j, 1:2], LN_EPS, 1.0, ALU.add, ALU.mult))
                nc.gpsimd.tensor_tensor(rstd[:, j, :], veps[:, j, :], minus_half[:], ALU.pow).then_inc(done, 1)

            def pool_product(t, s0, s1):
                n, heads = 2 * t + 2, POOL_HEADS[t]
                ch = heads * R
                k0 = TAPS - n
                s1 = min(s1, n)
                if s0 >= s1:
                    return
                pool.wait_ge(exp_ok, t + 1)
                pool.wait_ge(hist_ok, t + 1)
                pr = probs[:, t % 2, 0:LOGITS].rearrange("p (h k) -> p h k", h=HEADS)
                mark(nc.gpsimd.tensor_tensor(
                    prod_pool[:, s0:s1, 0:ch].rearrange("p s (h r) -> p s h r", r=R),
                    hist[:, s0:s1, D - ch:D].rearrange("p s (h r) -> p s h r", r=R),
                    pr[:, HEADS - heads:HEADS, k0 + s0:k0 + s1].rearrange("p h s -> p s h").unsqueeze(3).broadcast_to(
                        [P, s1 - s0, heads, R]), ALU.mult))

            def pool_sum(t):
                n, heads = 2 * t + 2, POOL_HEADS[t]
                ch = heads * R
                pool.wait_ge(pool_step, steps[0])
                while n > 1:
                    m = n // 2
                    low, high = prod_pool[:, 0:m, 0:ch], prod_pool[:, n - m:n, 0:ch]
                    link(nc.gpsimd.tensor_tensor(low, low, high, ALU.add))
                    n -= m
                pool.wait_ge(inv_ok, t + 1)
                if t >= 2:
                    pool.wait_ge(yT_ps, t - 1)
                nc.gpsimd.tensor_tensor(y[:, t % 2, D - ch:D].rearrange("p (h r) -> p h r", r=R),
                                        prod_pool[:, 0, 0:ch].rearrange("p (h r) -> p h r", r=R),
                                        inv_total[:, t % 2, HEADS - heads:HEADS].unsqueeze(2).broadcast_to(
                                            [P, heads, R]), ALU.mult).then_inc(y_pool_ok, 1)

            def result(t):
                pool.wait_ge(rstd_out, t + 1)
                if t >= 2:
                    pool.wait_ge(out_done[t % 2], 16 * (t // 2))
                link(nc.gpsimd.tensor_scalar(shift_out[:], mv[:, 2, 0:1], rstd[:, 2, :], -1.0, ALU.mult, ALU.mult))
                nc.gpsimd.tensor_scalar(res[:, t % 2, :], f[:, t % 3, :], rstd[:, 2, :], shift_out[:],
                                        ALU.mult, ALU.add).then_inc(res_ok, 1)

            def scale_h3(t):
                pool.wait_ge(centred_ok, t + 1)
                pool.wait_ge(rstd_mid, t + 1)
                if t >= 3:
                    pool.wait_ge(down_read, t - 2)
                nc.gpsimd.tensor_scalar(h3[:, t % 3, :], centred[:, t % 2, :], rstd[:, 1, 0:1], 1.0,
                                        ALU.mult, ALU.mult).then_inc(h3_ok, 1)

            def add_beta(t):
                if t == 0:
                    pool.wait_ge(ln_in, 16)
                pool.wait_ge(h1_ok, t + 1)
                nc.gpsimd.tensor_tensor(h1b[:, t % 2, :], h1b[:, t % 2, :], beta, ALU.add).then_inc(h1b_ok, 1)

            def weight_round(j, step, done):
                pool.wait_ge(wscale_ok, step)
                nc.gpsimd.tensor_scalar(w_raw[:, j, :], w_raw[:, j, :], w_scale[:, j:j + 1], MAGIC,
                                        ALU.mult, ALU.add).then_inc(done, 1)

            def weight_finish(j, ready, done):
                pool.wait_ge(ready, 1)
                nc.gpsimd.tensor_scalar(w_q[:, j, :], w_raw[:, j, :], -MAGIC, 1.0, ALU.add, ALU.mult).then_inc(done, 1)

            add_beta(0)
            pool_product(0, 0, 2)
            pool_sum(0)
            for i in range(1, TILES + 3):
                if i == 1:
                    weight_finish(0, wclip_gate, wq_gate_ok)
                if i == 2:
                    weight_round(2, 2, wround_down)
                if i < TILES:
                    add_beta(i)
                if i == 2:
                    weight_finish(2, wclip_down, wq_down_ok)
                first, second = SLOTS_FIRST if 1 < i < TILES else (0, 0)
                if i < TILES:
                    pool_product(i, 0, first)
                if i <= TILES:
                    inv_std(0, var_attn, rstd_attn, i - 1)
                if i < TILES:
                    pool_product(i, first, second)
                if i <= TILES:
                    inv_std(1, var_mid, rstd_mid, i - 1)
                if i < TILES:
                    pool_product(i, second, 2 * TILES)
                    pool_sum(i)
                if i >= 3:
                    inv_std(2, var_out, rstd_out, i - 3)
                    if i - 3 < TILES - 1:
                        result(i - 3)
                if i <= TILES:
                    scale_h3(i - 1)


_OUT = ("out_dram", (IMAGES, PATCHES, D))


def _lay_out(inputs):
    a = {n: np.asarray(v) for n, v in inputs.items()}

    def cols(w):
        o, i = w.shape
        return w.T.reshape(i // P, P, o).transpose(1, 0, 2)

    x = a["x"].reshape(IMAGES, CHANNELS, GRID, PATCH, GRID, PATCH).transpose(1, 3, 5, 0, 2, 4)
    x = x.reshape(KC_PATCH, P, TILES, P).transpose(2, 1, 0, 3)
    flat = lambda w: cols(w).reshape(P, -1)
    return {
        "xT": x,
        "tokW": cols(a["L0_tok_W"]),
        "w1": cols(a["L0_attn_w1"]),
        "ww": cols(a["L0_attn_ww"]),
        "w2": cols(a["L0_attn_w2"]),
        "wg": flat(a["L0_ffn_w_gate"]),
        "wu": flat(a["L0_ffn_w_up"]),
        "wd": flat(a["L0_ffn_w_down"]),
        "cols": np.stack([a["L0_tok_b"], a["L0_attn_b1"]]).reshape(2, KC, P).transpose(2, 0, 1),
        "bias": np.concatenate([a["L0_attn_bw"].reshape(-1), a["L0_attn_b2"].reshape(-1)]).reshape(1, LOGITS + D),
        "ln": np.concatenate([a["L0_attn_gamma"].reshape(-1), a["L0_attn_beta"].reshape(-1)]).reshape(1, 2 * D),
    }


def kernel(**inputs):
    import concourse.bacc as bacc
    from concourse.bass_utils import run_bass_kernel_spmd

    nc = bacc.Bacc("TRN2", target_bir_lowering=False, num_devices=1)
    arrays, args = {}, []
    for name, v in _lay_out(inputs).items():
        v = np.ascontiguousarray(v)
        arrays[f"in_{name}"] = v
        args.append(nc.dram_tensor(f"in_{name}", v.shape, mybir.dt.from_np(v.dtype), kind="ExternalInput").ap())
    name, shape = _OUT
    out = nc.dram_tensor(name, shape, mybir.dt.float32, kind="ExternalOutput").ap()
    vit_tower(nc, *args, out.rearrange("b n d -> (b n) d"))
    r = run_bass_kernel_spmd(nc, [arrays], core_ids=[0])
    return r.results[0][name]
```
